# Optimizing a Trainium2 kernel written in Bass

```python
import numpy as np
import jax
import jax.numpy as jnp

def _softmax(x, axis=-1):
    return jax.nn.softmax(x, axis=axis)

def _gelu(x):
    return jax.nn.gelu(x, approximate=True)

def _silu(x):
    return jax.nn.silu(x)

def _sigmoid(x):
    return jax.nn.sigmoid(x)

def _layernorm(x, axis=-1, eps=1e-05):
    m = jnp.mean(x, axis=axis, keepdims=True)
    v = jnp.var(x, axis=axis, keepdims=True)
    return (x - m) / jnp.sqrt(v + eps)

def _scatter_add(tgt, idx, src, axis=0):
    return tgt.at[idx].add(src)

def _segment_sum(src, seg, n):
    return jax.ops.segment_sum(src, seg, n)
kernel_name = 'mk_xattn_ffn_d1_seqx_r4_e2babb'

def setup_inputs(seed: int=0):
    np.random.seed(seed)
    _w = jnp.asarray

    def _rec_inputs():
        import jax
        import jax.numpy as jnp
        _rk = jax.random.key(seed)
        x = -0.0002928 + 1 * jax.random.normal(jax.random.fold_in(_rk, 1), (8, 512, 256), jnp.float32)
        _lenS = 512 - jax.random.randint(jax.random.fold_in(_rk, 7), (8,), 0, max(1, 512 // 4) + 1, jnp.int32)
        _lenS2 = 1601 - jax.random.randint(jax.random.fold_in(_rk, 8), (8,), 0, max(1, 1601 // 4) + 1, jnp.int32)
        _ctx_1024P = jax.random.normal(jax.random.fold_in(_rk, 11), (8, 16, 256), jnp.float32)
        _ctx_1024c = jax.random.dirichlet(jax.random.fold_in(_rk, 511), 0.3 * jnp.ones((16,), jnp.float32), (8, 1601))
        _ctx_1024t = jnp.einsum('bsk,bkd->bsd', _ctx_1024c, _ctx_1024P)
        _ctx_1024t = _ctx_1024t * jax.lax.rsqrt(jnp.mean(jnp.square(_ctx_1024t)) + 1e-12) * 0.953939
        ctx_1024 = -1.39393e-06 + 0.999914 * (_ctx_1024t + 0.3 * jax.random.normal(jax.random.fold_in(_rk, 611), (8, 1601, 256), jnp.float32))
        return (x, ctx_1024)
    x, ctx_1024 = _rec_inputs()

    def _L0_xattn_setup():
        import jax, jax.numpy as jnp
        import numpy as np
        EMBED_DIM = 256
        NUM_HEADS = 16
        HEAD_DIM = EMBED_DIM // NUM_HEADS
        key = jax.random.key(seed)
        ks = jax.random.split(key, 7)
        B, S, E = (2, 512, EMBED_DIM)
        bound = float(np.sqrt(6.0 / (E + E)))
        mkw = lambda k: jax.random.uniform(k, (E, E), jnp.float32, -bound, bound)
        return {'query': jax.random.normal(ks[0], (B, S, E), jnp.float32), 'key': jax.random.normal(ks[1], (B, S, E), jnp.float32), 'value': jax.random.normal(ks[2], (B, S, E), jnp.float32), 'Wq': mkw(ks[3]), 'Wk': mkw(ks[4]), 'Wv': mkw(ks[5]), 'Wo': mkw(ks[6])}
    _L0_xattn_all = _L0_xattn_setup()
    _L0_xattn_in = {k: v for k, v in _L0_xattn_all.items() if k in ('Wq', 'Wk', 'Wv', 'Wo')}
    del _L0_xattn_all

    def _L0_ffn_setup():
        import jax, jax.numpy as jnp
        import numpy as np
        B, S, D = (4, 1024, 256)
        E, F_EXP = (16, 512)
        F_C = 2.0
        F_SH = 512
        key = jax.random.key(seed)
        ks = jax.random.split(key, 8)
        s = 0.02
        return {'hidden_states': jax.random.normal(ks[0], (B, S, D), jnp.float32), 'gate_w': jax.random.normal(ks[1], (E, D), jnp.float32) * s, 'Wg': jax.random.normal(ks[2], (E, F_EXP, D), jnp.float32) * s, 'Wu': jax.random.normal(ks[3], (E, F_EXP, D), jnp.float32) * s, 'Wd': jax.random.normal(ks[4], (E, D, F_EXP), jnp.float32) * s, 'Ws_g': jax.random.normal(ks[5], (F_SH, D), jnp.float32) * s, 'Ws_u': jax.random.normal(ks[6], (F_SH, D), jnp.float32) * s, 'Ws_d': jax.random.normal(ks[7], (D, F_SH), jnp.float32) * s}
    _L0_ffn_all = _L0_ffn_setup()
    _L0_ffn_in = {k: v for k, v in _L0_ffn_all.items() if k in ('gate_w', 'Wg', 'Wu', 'Wd', 'Ws_g', 'Ws_u', 'Ws_d')}
    del _L0_ffn_all
    return {'x': x, 'ctx_1024': ctx_1024, 'L0_xattn_Wq': _L0_xattn_in['Wq'], 'L0_xattn_Wk': _L0_xattn_in['Wk'], 'L0_xattn_Wv': _L0_xattn_in['Wv'], 'L0_xattn_Wo': _L0_xattn_in['Wo'], 'L0_ffn_gate_w': _L0_ffn_in['gate_w'], 'L0_ffn_Wg': _L0_ffn_in['Wg'], 'L0_ffn_Wu': _L0_ffn_in['Wu'], 'L0_ffn_Wd': _L0_ffn_in['Wd'], 'L0_ffn_Ws_g': _L0_ffn_in['Ws_g'], 'L0_ffn_Ws_u': _L0_ffn_in['Ws_u'], 'L0_ffn_Ws_d': _L0_ffn_in['Ws_d']}

def reference(x, ctx_1024, L0_xattn_Wq, L0_xattn_Wk, L0_xattn_Wv, L0_xattn_Wo, L0_ffn_gate_w, L0_ffn_Wg, L0_ffn_Wu, L0_ffn_Wd, L0_ffn_Ws_g, L0_ffn_Ws_u, L0_ffn_Ws_d):
    import jax
    import jax.numpy as jnp

    def _L0_xattn_ref(query, key, value, Wq, Wk, Wv, Wo):
        import jax, jax.numpy as jnp
        import numpy as np
        EMBED_DIM = 256
        NUM_HEADS = 16
        HEAD_DIM = EMBED_DIM // NUM_HEADS
        B, L, E = query.shape
        H, D = (NUM_HEADS, HEAD_DIM)
        scale = D ** (-0.5)
        q = (query @ Wq.T).reshape(B, L, H, D) * scale
        k = (key @ Wk.T).reshape(B, -1, H, D)
        v = (value @ Wv.T).reshape(B, -1, H, D)
        scores = jax.nn.sigmoid(jnp.einsum('blhd,bshd->bhls', q, k))
        o = jnp.einsum('bhls,bshd->blhd', scores, v).reshape(B, L, E)
        return o @ Wo.T

    def _L0_ffn_ref(hidden_states, gate_w, Wg, Wu, Wd, Ws_g, Ws_u, Ws_d):
        import jax, jax.numpy as jnp
        import numpy as np
        B, S, D = (4, 1024, 256)
        E, F_EXP = (16, 512)
        F_C = 2.0
        F_SH = 512
        b, s, d = hidden_states.shape
        e = gate_w.shape[0]
        cap = int(s * F_C / e)
        logits = jnp.einsum('bsd,ed->bse', hidden_states, gate_w)
        scores = jax.nn.softmax(logits, axis=-1).transpose(0, 2, 1)
        topk_w, topk_idx = jax.lax.top_k(scores, cap)
        x_tok = jnp.take_along_axis(hidden_states[:, None, :, :], topk_idx[..., None], axis=2)
        g = jnp.einsum('becd,efd->becf', x_tok, Wg)
        u = jnp.einsum('becd,efd->becf', x_tok, Wu)
        h = jax.nn.gelu(g, approximate=False) * u
        eo = jnp.einsum('becf,edf->becd', h, Wd) * topk_w[..., None]
        offs = (jnp.arange(b) * s)[:, None, None]
        flat_idx = (topk_idx + offs).reshape(-1)
        flat = jnp.zeros((b * s, d), hidden_states.dtype)
        flat = flat.at[flat_idx].add(eo.reshape(-1, d))
        out = flat.reshape(b, s, d)
        gs = jnp.einsum('bsd,fd->bsf', hidden_states, Ws_g)
        us = jnp.einsum('bsd,fd->bsf', hidden_states, Ws_u)
        shared = jnp.einsum('bsf,df->bsd', jax.nn.gelu(gs, approximate=False) * us, Ws_d)
        return out + shared
    x = x + _L0_xattn_ref(_layernorm(x, axis=-1), ctx_1024, ctx_1024, L0_xattn_Wq, L0_xattn_Wk, L0_xattn_Wv, L0_xattn_Wo)
    x = x + _L0_ffn_ref(_layernorm(x, axis=-1), L0_ffn_gate_w, L0_ffn_Wg, L0_ffn_Wu, L0_ffn_Wd, L0_ffn_Ws_g, L0_ffn_Ws_u, L0_ffn_Ws_d)
    return x

_drawn_inputs = setup_inputs


def setup_inputs(seed=0):
    import zlib

    import numpy as np

    out = dict(_drawn_inputs(seed))
    spreads = {}
    factors = {'L0_ffn_gate_w': 35.734,
     'L0_ffn_Wg': 39.435,
     'L0_ffn_Wu': 32.223,
     'L0_ffn_Wd': 33.429,
     'L0_ffn_Ws_g': 21.642,
     'L0_ffn_Ws_u': 8.0,
     'L0_ffn_Ws_d': 8.0}
    for name, (base, spread) in spreads.items():
        noise = np.random.default_rng([zlib.crc32(name.encode()), seed]).standard_normal(out[name].shape)
        drawn = base * np.exp(spread * noise) if base else spread * noise
        out[name] = jnp.asarray(drawn.astype(out[name].dtype))
    for name, factor in factors.items():
        out[name] = (out[name] * factor).astype(out[name].dtype)
    return out
```

```python
from contextlib import ExitStack

import concourse.bass as bass
from concourse import mybir
from concourse.alu_op_type import AluOpType as ALU

F32 = mybir.dt.float32
F32R = mybir.dt.float32r
BF16 = mybir.dt.bfloat16
I32 = mybir.dt.int32
U32 = mybir.dt.uint32
ACT = mybir.ActivationFunctionType
AX_X = mybir.AxisListType.X

P = 128
B, S, D = 8, 512, 256
T = 1601
TP = T + 1
H, HD = 16, 16
HALF = H // 2
KC = D // P
TT = S // P
NST = -(-T // P)
QUADS = 2 * NST
GROUPS = 2 * QUADS
CHUNK = 512
NCH = -(-T // CHUNK)
RING = 4
LAG = 2
STEPS = 2 * B
SCALE = HD ** -0.5

E, F, CAP = 16, 512, 64
FT = F // P
SETS = E + 1
UNITS = B + E
EPS = 1e-5

KEY_PART = (0, 0, 1, 1, 0, 2)
QUERY_PART = (0, 1, 0, 1, 2, 0)
STACK = HD * len(KEY_PART)
STACK_DMAS = 16 * len(KEY_PART)

PREP = 2 * NCH + 1
POST = 2 + KC + 1
WQ, WK, WV, WO = range(4)


def key_rows(st):
    return min(P, T - P * st)


def chunk_of(kc):
    s0 = CHUNK * kc
    return s0, min(CHUNK, TP - s0), range(s0 // P, min(NST, (s0 + CHUNK) // P))


def score_slot(half, k):
    return (k + (half == 0)) % 3


def probs_slot(half, q):
    return (q + (2 if half == 0 else 0)) % RING


MISC_LOOP = 2 * PREP + KC
MISC_TURN = 2 * PREP + KC + POST


def keys_loaded(half, batches):
    if isinstance(batches, int) and batches == 0:
        return 0
    return STACK_DMAS * (batches + (NCH - 1 if half == 0 else 0))


class Count:

    def __init__(self, base=0):
        self.base, self.n = base, 0

    def up(self):
        self.n += 1
        return 1

    def now(self):
        return self.base + self.n


def wait_past(engine, sem, value):
    if not isinstance(value, int) or value > 0:
        engine.wait_ge(sem, value)


def wait_apart(engine, reached, *waits):
    waits = [(sem, value) for sem, value in waits if not isinstance(value, int) or value > 0]
    values = [value if isinstance(value, int) else engine.compute_val(value) for _, value in waits]
    engine.wait_ge(*reached)
    for (sem, _), value in zip(waits, values):
        engine.wait_ge(sem, value)


def at(i):
    return bass.ds(i, 1)


def build(nc, x, ctx_t, w_attn, gate_t, w_gu, w_d, out):
    with ExitStack() as keep:
        def sem(name):
            return keep.enter_context(nc.semaphore(name))

        def dram(name, shape, dt):
            return nc.dram_tensor(name, shape, dt, kind="Internal").ap()

        def sbuf(stack):
            return lambda name, shape, dt=F32: stack.enter_context(nc.sbuf_tensor(name, shape, dt))

        key_scr = [dram(f"key_scr{g}", (3, P, TP), BF16) for g in range(2)]
        query_scr = [dram(f"query_scr{g}", (3, P, S), BF16) for g in range(2)]
        resid_scr = dram("resid_scr", (B, P, TT, D), F32)
        norm_scr = dram("norm_scr", (B * S, D), F32)
        norm_t_scr = dram("norm_t_scr", (2, B, P, KC, S), F32)

        sb = sbuf(keep)
        w_hi = sb("w_hi", [P, 4, KC, D], F32R)
        w_lo = sb("w_lo", [P, 4, KC, D], F32R)
        gate_raw = sb("gate_raw", [P, KC, E])
        gate_hi = sb("gate_hi", [P, KC, E], F32R)
        gate_lo = sb("gate_lo", [P, KC, E], F32R)
        ident = sb("ident", [P, P])
        o_hi = sb("o_hi", [P, 2, S], F32R)
        o_lo = sb("o_lo", [P, 2, S], F32R)
        xn = sb("xn", [P, TT, D])
        resid = sb("resid", [P, TT, D])
        norm = sb("norm", [P, TT, D])
        nt_hi = sb("nt_hi", [P, KC, S], F32R)
        nt_lo = sb("nt_lo", [P, KC, S], F32R)
        logits = sb("logits", [P, TT, B, E])
        bn = sb("bn", [P, TT, nc.vector.BN_STATS_DIM])
        mv = sb("mv", [P, TT, nc.vector.BN_AGGR_DIM])
        var = sb("var", [P, TT])
        rs_bits = sb("rs_bits", [P, TT], I32)
        rs = sb("rs", [P, TT])
        rs_sq = sb("rs_sq", [P, TT])
        rs_c = sb("rs_c", [P, TT])
        part_iota = sb("part_iota", [P, 1], I32)
        part_batch = sb("part_batch", [P, 1], I32)
        row_base_i = sb("row_base_i", [P, 1], I32)
        row_base = sb("row_base", [P, 1])
        row_max = sb("row_max", [P, TT * B])
        row_sum = sb("row_sum", [P, TT * B])
        row_inv = sb("row_inv", [P, TT * B])
        sum4 = sb("sum4", [P, TT * B, 4])
        sum2 = sb("sum2", [P, TT * B, 2])
        top_w = sb("top_w", [P, 2, CAP])
        top_i = sb("top_i", [P, CAP], U32)
        top_row = sb("top_row", [P, 2, CAP])
        slot_row = sb("slot_row", [P, TT, E], U32)
        slot_w = sb("slot_w", [P, TT, E])
        gather_row = [sb(f"gather_row{p}", [P, TT], U32) for p in range(2)]
        add_row = [sb(f"add_row{p}", [P, TT], U32) for p in range(2)]
        add_w = [sb(f"add_w{p}", [P, TT]) for p in range(2)]

        with ExitStack() as stage_a:
            sa = sbuf(stage_a)
            keys0 = sa("keys0", [STACK, HALF, TP + 2], BF16)
            values0 = sa("values0", [P, NST, 4, 2, 2 * HD])
            queries0 = sa("queries0", [STACK, HALF, S], BF16)
            ctx_raw = [sa(f"ctx_raw{i}", [P, KC, CHUNK]) for i in range(2)]
            ctx_hi = sa("ctx_hi", [P, KC, CHUNK], F32R)
            ctx_lo = sa("ctx_lo", [P, KC, CHUNK], F32R)
            key_parts = [sa(f"key_parts{i}", [P, 3, CHUNK], BF16) for i in range(2)]
            query_parts = sa("query_parts", [P, 3, S], BF16)
            rest = sa("rest", [P, CHUNK])
            probs = sa("probs", [P, RING, 4, S])
            keys = [keys0, sa("keys1", [STACK, HALF, TP + 2], BF16)]
            values = [values0, sa("values1", [P, NST, 4, 2, 2 * HD])]
            queries = [queries0, sa("queries1", [STACK, HALF, S], BF16)]

        with ExitStack() as stage_b:
            sb = sbuf(stage_b)
            gu_raw = [sb(f"gu_raw{i}", [P, 2, KC, F]) for i in range(2)]
            d_raw = [sb(f"d_raw{i}", [P, FT, D]) for i in range(2)]
            gu_hi0 = sb("gu_hi0", [P, 2, KC, F], F32R)
            gu_lo0 = sb("gu_lo0", [P, 2, KC, F], F32R)
            d_hi0 = sb("d_hi0", [P, FT, D], F32R)
            d_lo0 = sb("d_lo0", [P, FT, D], F32R)
            tok_hi = [sb(f"tok_hi{i}", [P, KC, S], F32R) for i in range(2)]
            tok_lo = [sb(f"tok_lo{i}", [P, KC, S], F32R) for i in range(2)]
            gu_hi = [gu_hi0, sb("gu_hi1", [P, 2, KC, F], F32R)]
            gu_lo = [gu_lo0, sb("gu_lo1", [P, 2, KC, F], F32R)]
            d_hi = [d_hi0, sb("d_hi1", [P, FT, D], F32R)]
            d_lo = [d_lo0, sb("d_lo1", [P, FT, D], F32R)]
            gathered = [sb(f"gathered{i}", [P, TT, D]) for i in range(2)]
            gelu = sb("gelu", [P, 2, S])
            hidden = sb("hidden", [P, 2, S])
            hid_hi = [sb(f"hid_hi{i}", [P, FT, S], F32R) for i in range(2)]
            hid_lo = [sb(f"hid_lo{i}", [P, FT, S], F32R) for i in range(2)]
            result = [sb(f"result{i}", [P, TT, D]) for i in range(2)]
            resid_in = [sb(f"resid_in{i}", [P, TT, D]) for i in range(2)]
            choice = sb("choice", [P, S])

        score = [keep.enter_context(nc.psum_tensor(f"score{i}", [P, 2, S], F32)) for i in range(3)]
        acc = keep.enter_context(nc.psum_tensor("acc", [P, S], F32))
        misc = keep.enter_context(nc.psum_tensor("misc", [P, S], F32))
        g_bank, u_bank, d_bank, t_bank = score[0], score[1], score[2], [acc, misc]

        const_ready = sem("const_ready")
        attn_w_in = sem("attn_w_in")
        w_split = sem("w_split")
        ctx_in = [sem(f"ctx_in{i}") for i in range(2)]
        ctx_split = sem("ctx_split")
        x_in = sem("x_in")
        x_again_in = sem("x_again_in")
        ln_step = sem("ln_step")
        xn_ready = sem("xn_ready")
        norm_ready = sem("norm_ready")
        split_step = sem("split_step")
        misc_full = sem("misc_full")
        misc_copied = sem("misc_copied")
        key_parts_ready = sem("key_parts_ready")
        key_written = [sem(f"key_written{i}") for i in range(2)]
        keys_in = [sem(f"keys_in{g}") for g in range(2)]
        query_parts_ready = sem("query_parts_ready")
        query_written = sem("query_written")
        queries_in = [sem(f"queries_in{g}") for g in range(2)]
        scores_done = sem("scores_done")
        probs_done = sem("probs_done")
        quad_done = sem("quad_done")
        acc_copied = sem("acc_copied")
        post_stored = sem("post_stored")

        set_in = [sem(f"set_in{i}") for i in range(2)]
        set_hi = sem("set_hi")
        set_split = sem("set_split")
        tok_in = [sem(f"tok_in{i}") for i in range(2)]
        resid_read = [sem(f"resid_read{i}") for i in range(2)]
        g_full = sem("g_full")
        u_full = sem("u_full")
        gelu_done = sem("gelu_done")
        hidden_done = sem("hidden_done")
        hid_split = sem("hid_split")
        d_full = sem("d_full")
        d_copied = sem("d_copied")
        tok_full = sem("tok_full")
        tok_copied = sem("tok_copied")
        tok_step = sem("tok_step")
        soft_step = sem("soft_step")
        exp_done = sem("exp_done")
        rows_ready = sem("rows_ready")
        adds_ready = sem("adds_ready")
        rows_in = [sem(f"rows_in{i}") for i in range(2)]
        shared_out = [sem(f"shared_out{i}") for i in range(2)]
        added = [sem(f"added{i}") for i in range(2)]
        SHARED_OUT = 16 * (B // 2)

        W2 = (w_hi, w_lo)
        PRODUCTS = ((0, 0), (0, 1), (1, 0))
        STORE = 64

        block = keep.enter_context(nc.Block())

        @block.sync
        def _(sp):
            sp.dma_start(probs[:, 0, :, :].rearrange("p w (k d) -> p w k d", k=KC),
                         w_attn.rearrange("w (k p) d -> p w k d", p=P)).then_inc(attn_w_in, 16)
            sp.dma_start(gate_raw[:], gate_t.rearrange("(k p) e -> p k e", p=P)).then_inc(attn_w_in, 16)

            def key_stack(prep, half, batch):
                for kc in range(NCH):
                    s0, n, _ = chunk_of(kc)
                    wait_apart(sp, (attn_w_in, 32), (key_parts_ready, NCH * prep + kc + 1),
                               *([(keys_in[half], keys_loaded(half, batch))] if kc == 0 else []))
                    sp.dma_start(key_scr[half][:, :, s0:s0 + n].rearrange("j p s -> p j s"),
                                 key_parts[kc % 2][:, :, 0:n]).then_inc(key_written[kc % 2], 16)
                wait_apart(sp, (attn_w_in, 32),
                           (key_written[0], 16 * (NCH // 2) * (prep + 1)),
                           (key_written[1], 16 * (NCH // 2) * (prep + 1)),
                           (scores_done, GROUPS * (prep - 1)))
                for j, part in enumerate(KEY_PART):
                    sp.dma_start(keys[half][HD * j:HD * (j + 1), :, 0:TP],
                                 key_scr[half][part].rearrange("(h r) s -> r h s", r=HD)
                                 ).then_inc(keys_in[half], 16)

            def query_stack(prep, half, batch):
                wait_apart(sp, (attn_w_in, 32), (query_parts_ready, prep + 1),
                           (queries_in[half], STACK_DMAS * batch))
                sp.dma_start(query_scr[half].rearrange("j p s -> p j s"),
                             query_parts[:]).then_inc(query_written, 16)
                wait_apart(sp, (attn_w_in, 32), (query_written, 16 * (prep + 1)))
                for j, part in enumerate(QUERY_PART):
                    sp.dma_start(queries[half][HD * j:HD * (j + 1), :, :],
                                 query_scr[half][part].rearrange("(h r) s -> r h s", r=HD)
                                 ).then_inc(queries_in[half], 16)

            def store_batch(b, misc_count):
                wait_apart(sp, (attn_w_in, 32), (norm_ready, b + 1))
                sp.dma_start(resid_scr[at(b)].rearrange("o p t d -> p (o t) d"),
                             resid[:]).then_inc(post_stored, 16)
                sp.dma_start(norm_scr.rearrange("(b t p) d -> b p t d", b=B, p=P)[at(b)]
                             .rearrange("o p t d -> p (o t) d"), norm[:]).then_inc(post_stored, 16)
                wait_apart(sp, (attn_w_in, 32), (misc_copied, misc_count))
                for part, tile in enumerate((nt_hi, nt_lo)):
                    sp.dma_start(norm_t_scr[part][at(b)].rearrange("o p k s -> p (o k) s"),
                                 tile[:].bitcast(F32)).then_inc(post_stored, 16)

            def load_resid_a(batch):
                sp.dma_start(resid[:], x.rearrange("(b t p) d -> b p t d", b=B, p=P)[at(batch)]
                             .rearrange("o p t d -> p (o t) d")).then_inc(x_again_in, 16)

            for kc in range(NCH):
                s0, n, _ = chunk_of(kc)
                sp.wait_ge(key_parts_ready, kc + 1)
                sp.dma_start(key_scr[0][:, :, s0:s0 + n].rearrange("j p s -> p j s"),
                             key_parts[kc % 2][:, :, 0:n]).then_inc(key_written[kc % 2], 16)
                sp.wait_ge(key_written[kc % 2], 16 * (kc // 2 + 1))
                if kc:
                    sp.wait_ge(keys_in[0], STACK_DMAS * kc)
                for j, part in enumerate(KEY_PART):
                    sp.dma_start(keys[0][HD * j:HD * (j + 1), :, s0:s0 + n],
                                 key_scr[0][part][:, s0:s0 + n].rearrange("(h r) s -> r h s", r=HD)
                                 ).then_inc(keys_in[0], 16)
            load_resid_a(0)
            query_stack(1, 1, 0)
            key_stack(1, 1, 0)
            with sp.Fori(0, B - 1) as i:
                key_stack(2 * i + 2, 0, i + 1)
                query_stack(2 * i + 2, 0, i + 1)
                key_stack(2 * i + 3, 1, i + 1)
                query_stack(2 * i + 3, 1, i + 1)
                store_batch(i, MISC_LOOP + MISC_TURN * i + 2 * PREP + KC + 2 + KC)
                wait_apart(sp, (attn_w_in, 32), (post_stored, STORE * (i + 1)))
                load_resid_a(i + 1)

            def load_weights(s, slot):
                sp.dma_start(gu_raw[slot][:].rearrange("p w k f -> p (w k) f"),
                             w_gu[at(s)].rearrange("o w (k p) f -> p (o w k) f", p=P)
                             ).then_inc(set_in[slot], 16)
                sp.dma_start(d_raw[slot][:], w_d[at(s)].rearrange("o (t p) d -> p (o t) d", p=P)
                             ).then_inc(set_in[slot], 16)

            def load_tokens(b):
                for part, tile in enumerate((tok_hi, tok_lo)):
                    sp.dma_start(tile[b % 2][:].bitcast(F32), norm_t_scr[part][b]).then_inc(tok_in[b % 2], 16)

            def load_resid(b):
                sp.dma_start(resid_in[b % 2][:], resid_scr[b]).then_inc(resid_read[b % 2], 16)

            sp.wait_ge(quad_done, QUADS * (STEPS - 1))
            for half in range(2):
                sp.wait_ge(keys_in[half], keys_loaded(half, B))
                sp.wait_ge(queries_in[half], STACK_DMAS * B)
            load_weights(0, 0)
            sp.wait_ge(post_stored, STORE * (B - 1))
            load_tokens(0)
            load_tokens(1)
            load_weights(1, 1)
            sp.wait_ge(quad_done, QUADS * STEPS)
            load_resid(0)
            load_resid(1)
            store_batch(B - 1, MISC_LOOP + MISC_TURN * (B - 1) + 2 + KC)

            def store_unit(n):
                sp.wait_ge(d_copied, 2 * n + 2)
                sp.dma_start(out.rearrange("(b t p) d -> b p t d", b=B, p=P)[n],
                             result[n % 2][:]).then_inc(shared_out[n % 2], 16)

            for n in range(1, B + 1):
                if n + 1 < B:
                    if n + 1 == B - 1:
                        sp.wait_ge(post_stored, STORE * B)
                    sp.wait_ge(u_full, FT * n)
                    load_tokens(n + 1)
                store_unit(n - 1)
                if n + 1 < B:
                    load_resid(n + 1)
                if n == B - 1:
                    sp.wait_ge(set_split, 2)
                    load_weights(2, 0)

            def load_ahead(s, slot):
                wait_apart(sp, (attn_w_in, 32), (set_split, 2 * s - 2))
                load_weights(s, slot)

            load_ahead(3, 1)
            with sp.Fori(0, (E - 4) // 2) as i:
                load_ahead(2 * i + 4, 0)
                load_ahead(2 * i + 5, 1)
            load_ahead(SETS - 1, (SETS - 1) % 2)
            for i in range(2):
                sp.wait_ge(added[i], 16 * TT * (E // 2))

        @block.gpsimd
        def _(pool):
            def load_ctx(prep, batch, chunks=range(NCH)):
                for kc in chunks:
                    s0, n, _ = chunk_of(kc)
                    if not (isinstance(prep, int) and prep == 0 and kc < 2):
                        wait_apart(pool, (x_in, 16), (ctx_split, 2 * NCH * prep + 2 * kc - 2))
                    pool.dma_start(ctx_raw[kc % 2][:, :, 0:n],
                                   ctx_t[at(batch)].rearrange("o (k p) s -> p (o k) s", p=P)
                                   [:, :, s0:s0 + n]).then_inc(ctx_in[kc % 2], 16)

            x_rows = x.rearrange("(b t p) d -> b p t d", b=B, p=P)

            pool.dma_start(xn[:], x_rows[0]).then_inc(x_in, 16)
            load_ctx(0, 0, range(2))
            pool.memset(ident[:], 0.0).then_inc(const_ready, 1)
            pool.iota(part_iota[:], pattern=[[0, 1]], base=0, channel_multiplier=1
                      ).then_inc(const_ready, 1)
            pool.wait_ge(const_ready, 1)
            pool.affine_select(out=ident[:], in_=ident[:], compare_op=ALU.not_equal, fill=1.0, base=0,
                               pattern=[[-1, P]], channel_multiplier=1).then_inc(const_ready, 1)
            pool.memset(values[0][:], 0.0).then_inc(const_ready, 1)
            pool.memset(values[1][:], 0.0).then_inc(const_ready, 1)
            load_ctx(0, 0, range(2, NCH))
            load_ctx(1, 0)
            with pool.Fori(0, B - 1) as i:
                wait_apart(pool, (x_in, 16), (query_parts_ready, 2 * i + 1))
                pool.dma_start(xn[:], x_rows[at(i + 1)].rearrange("o p t d -> p (o t) d")
                               ).then_inc(x_in, 16)
                load_ctx(2 * i + 2, i + 1)
                load_ctx(2 * i + 3, i + 1)

            def split_lo(which, slot, s):
                pool.wait_ge(set_hi, 2 * s + which + 1)
                raw, hi, lo = ((gu_raw, gu_hi, gu_lo), (d_raw, d_hi, d_lo))[which]
                flat = "p w k f -> p (w k f)" if which == 0 else "p t d -> p (t d)"
                pool.tensor_tensor(lo[slot][:].rearrange(flat), raw[slot][:].rearrange(flat),
                                   hi[slot][:].rearrange(flat).bitcast(F32), ALU.subtract
                                   ).then_inc(set_split, 1)

            pool.wait_ge(set_in[0], 32)
            pool.tensor_copy(gu_hi[0][:].rearrange("p w k f -> p (w k f)"),
                             gu_raw[0][:].rearrange("p w k f -> p (w k f)")).then_inc(set_hi, 1)
            split_lo(0, 0, 0)
            pool.tensor_copy(d_hi[0][:].rearrange("p t d -> p (t d)"),
                             d_raw[0][:].rearrange("p t d -> p (t d)")).then_inc(set_hi, 1)
            split_lo(1, 0, 0)

            def gather(e, par, before):
                wait_apart(pool, (post_stored, STORE * B), (rows_ready, e + 1),
                           *([(tok_full, TABLES + KC * (e - 1))] if before else []))
                for t in range(TT):
                    pool.indirect_dma_start(
                        gathered[par][:, t, :], None, norm_scr[:, :],
                        bass.IndirectOffsetOnAxis(ap=gather_row[par][:, t:t + 1], axis=0)
                    ).then_inc(rows_in[par], 16)

            def add_rows(e, par):
                wait_apart(pool, (shared_out[0], SHARED_OUT), (shared_out[1], SHARED_OUT),
                           (adds_ready, 2 * e + 2), (d_copied, 2 * (B + e) + 2),
                           (added[1 - par], 8 * TT * (e + par)))
                for t in range(TT):
                    pool.indirect_dma_start(
                        out[:, :], bass.IndirectOffsetOnAxis(ap=add_row[par][:, t:t + 1], axis=0),
                        result[par][:, t, :], None, compute_op=ALU.add
                    ).then_inc(added[par], 16)

            gather(0, 0, False)
            split_lo(0, 1, 1)
            gather(1, 1, False)
            split_lo(1, 1, 1)

            def beside_unit(e, par, add, more_sets, more_rows):
                if more_sets:
                    split_lo(0, par, e + 2)
                if more_rows:
                    gather(e + 2, par, True)
                if add:
                    add_rows(e - 1, 1 - par)
                if more_sets:
                    split_lo(1, par, e + 2)

            beside_unit(0, 0, False, True, True)
            beside_unit(1, 1, True, True, True)
            with pool.Fori(0, (E - 4) // 2) as i:
                beside_unit(2 * i + 2, 0, True, True, True)
                beside_unit(2 * i + 3, 1, True, True, True)
            beside_unit(E - 2, 0, True, True, False)
            beside_unit(E - 1, 1, True, False, False)
            add_rows(E - 1, 1)

        @block.scalar
        def _(act):
            def sigmoids(step, half):
                for k in range(GROUPS):
                    q, pair = divmod(k, 2)
                    n = key_rows(q // 2)
                    act.wait_ge(scores_done, GROUPS * step + k + 1)
                    if pair == 0:
                        wait_past(act, quad_done, QUADS * step + q - RING + 1)
                    act.activation(probs[0:n, probs_slot(half, q), 2 * pair:2 * pair + 2, :],
                                   score[score_slot(half, k)][0:n, :, :], ACT.Sigmoid, scale=SCALE
                                   ).then_inc(probs_done, 1)

            act.wait_ge(query_parts_ready, 1)
            act.dma_start(query_scr[0].rearrange("j p s -> p j s"), query_parts[:]
                          ).then_inc(query_written, 16)
            act.wait_ge(query_written, 16)
            for j, part in enumerate(QUERY_PART):
                act.dma_start(queries[0][HD * j:HD * (j + 1), :, :],
                              query_scr[0][part].rearrange("(h r) s -> r h s", r=HD)
                              ).then_inc(queries_in[0], 16)
            sigmoids(0, 0)
            with act.Fori(0, B - 1) as i:
                sigmoids(2 * i + 1, 1)
                sigmoids(2 * i + 2, 0)
            sigmoids(STEPS - 1, 1)

            def gelus(n, quarters):
                for f in quarters:
                    act.wait_ge(g_full, FT * n + f + 1)
                    wait_past(act, hidden_done, FT * n + f - 1)
                    act.activation(gelu[:, f % 2, :], g_bank[:, f % 2, :], ACT.Gelu
                                   ).then_inc(gelu_done, 1)

            def hi_parts(which, slot, s, last_unit):
                if which == 0:
                    act.wait_ge(set_in[slot], 16 * (s - slot) + 32)
                    if last_unit is not None:
                        act.wait_ge(u_full, FT * (last_unit + 1))
                    act.activation(gu_hi[slot][:].rearrange("p w k f -> p (w k f)"),
                                   gu_raw[slot][:].rearrange("p w k f -> p (w k f)"), ACT.Copy
                                   ).then_inc(set_hi, 1)
                else:
                    if last_unit is not None:
                        act.wait_ge(d_full, 2 * (last_unit + 1))
                    act.activation(d_hi[slot][:].rearrange("p t d -> p (t d)"),
                                   d_raw[slot][:].rearrange("p t d -> p (t d)"), ACT.Copy
                                   ).then_inc(set_hi, 1)

            for n in range(B):
                gelus(n, (0, 1))
                if n == 2:
                    act.wait_ge(soft_step, SOFT_SUB)
                    act.activation(logits[:].rearrange("p t b e -> p (t b e)"),
                                   logits[:].rearrange("p t b e -> p (t b e)"), ACT.Exp
                                   ).then_inc(exp_done, 1)
                if n == B - 1:
                    hi_parts(0, 1, 1, None)
                gelus(n, (2, 3))
                if n == B - 1:
                    hi_parts(1, 1, 1, None)

            def expert(e, par, more_sets):
                n = e + B
                gelus(n, (0, 1))
                if more_sets:
                    hi_parts(0, par, e + 2, n - 1)
                gelus(n, (2, 3))
                if more_sets:
                    hi_parts(1, par, e + 2, n - 1)

            expert(0, 0, True)
            expert(1, 1, True)
            with act.Fori(0, (E - 4) // 2) as i:
                expert(2 * i + 2, 0, True)
                expert(2 * i + 3, 1, True)
            expert(E - 2, 0, True)
            expert(E - 1, 1, False)

        @block.vector
        def _(dve):
            m = Count()
            s = Count()
            ln = Count()

            def split_ctx(prep, kc):
                _, n, _ = chunk_of(kc)
                done = 2 * NCH * prep + 2 * kc
                dve.wait_ge(ctx_in[kc % 2], 16 * (NCH // 2 * prep + kc // 2 + 1))
                dve.tensor_copy(ctx_hi[:, :, 0:n], ctx_raw[kc % 2][:, :, 0:n]).then_inc(ctx_split, 1)
                dve.wait_ge(ctx_split, done + 1)
                dve.tensor_tensor(ctx_lo[:, :, 0:n], ctx_raw[kc % 2][:, :, 0:n],
                                  ctx_hi[:, :, 0:n].bitcast(F32), ALU.subtract).then_inc(ctx_split, 1)

            def three_parts(parts, n, ready):
                dve.wait_ge(misc_full, m.now() + 1)
                dve.tensor_copy(parts[:, 0, 0:n], misc[:, 0:n]).then_inc(split_step, s.up())
                dve.wait_ge(split_step, s.now())
                dve.tensor_tensor(rest[:, 0:n], misc[:, 0:n], parts[:, 0, 0:n], ALU.subtract
                                  ).then_inc(misc_copied, m.up())
                dve.wait_ge(misc_copied, m.now())
                dve.tensor_copy(parts[:, 1, 0:n], rest[:, 0:n]).then_inc(split_step, s.up())
                dve.wait_ge(split_step, s.now())
                dve.tensor_tensor(parts[:, 2, 0:n], rest[:, 0:n], parts[:, 1, 0:n], ALU.subtract
                                  ).then_inc(ready, 1)

            def key_chunk(prep, kc):
                _, n, _ = chunk_of(kc)
                wait_past(dve, key_written[kc % 2], 16 * (NCH // 2 * prep + kc // 2))
                three_parts(key_parts[kc % 2], n, key_parts_ready)

            def value_chunk(prep, half, kc):
                _, _, tiles = chunk_of(kc)
                n, rows = len(tiles), key_rows(tiles[0])
                dve.wait_ge(misc_full, m.now() + 1)
                if kc == 0:
                    wait_past(dve, quad_done, QUADS * (prep - 1))
                to = values[half][0:rows, tiles[0]:tiles[0] + n, :, :, :].rearrange(
                    "p t c e (g r) -> p (t c) (e g) r", g=2)[:, :, 0::3, :]
                dve.tensor_copy(to, misc[0:rows, 0:P * n].rearrange(
                    "p (tc e r) -> p tc e r", e=2, r=HD)).then_inc(misc_copied, m.up())

            def two_parts(hi, lo):
                dve.wait_ge(misc_full, m.now() + 1)
                dve.tensor_copy(hi, misc[:]).then_inc(split_step, s.up())
                dve.wait_ge(split_step, s.now())
                dve.tensor_tensor(lo, misc[:], hi.bitcast(F32), ALU.subtract
                                  ).then_inc(misc_copied, m.up())

            def query_chunk(prep):
                wait_past(dve, query_written, 16 * prep)
                three_parts(query_parts, S, query_parts_ready)

            def layer_norm(to, of, ready):
                for t in range(TT):
                    dve.bn_stats(bn[:, t, :], of[:, t, :]).then_inc(ln_step, ln.up())
                wait_apart(dve, (x_in, 16), (ln_step, ln.now()))
                for t in range(TT):
                    dve.bn_aggr(mv[:, t, :], bn[:, t, :]).then_inc(ln_step, ln.up())
                dve.wait_ge(ln_step, ln.now())
                dve.tensor_scalar(var[:], mv[:, :, 1], EPS, None, ALU.add).then_inc(ln_step, ln.up())
                dve.wait_ge(ln_step, ln.now())
                dve.tensor_scalar(rs_bits[:], var[:].bitcast(I32), 1, None, ALU.logical_shift_right
                                  ).then_inc(ln_step, ln.up())
                dve.wait_ge(ln_step, ln.now())
                dve.tensor_scalar(rs[:].bitcast(I32), rs_bits[:], -1.0, float(0x5F3759DF),
                                  ALU.mult, ALU.add).then_inc(ln_step, ln.up())
                for _ in range(3):
                    dve.wait_ge(ln_step, ln.now())
                    dve.tensor_tensor(rs_sq[:], rs[:], rs[:], ALU.mult).then_inc(ln_step, ln.up())
                    dve.wait_ge(ln_step, ln.now())
                    dve.scalar_tensor_tensor(out=rs_c[:], in0=rs_sq[:], scalar=-0.5, in1=var[:],
                                             op0=ALU.mult, op1=ALU.mult).then_inc(ln_step, ln.up())
                    dve.wait_ge(ln_step, ln.now())
                    dve.scalar_tensor_tensor(out=rs[:], in0=rs_c[:], scalar=1.5, in1=rs[:],
                                             op0=ALU.add, op1=ALU.mult).then_inc(ln_step, ln.up())
                dve.wait_ge(ln_step, ln.now())
                for t in range(TT):
                    last = dve.tensor_scalar(to[:, t, :], of[:, t, :], mv[:, t, 0:1], rs[:, t:t + 1],
                                             ALU.subtract, ALU.mult)
                last.then_inc(ready, 1)

            def attention_out(step, half):
                dve.wait_ge(quad_done, QUADS * (step + 1))
                dve.tensor_copy(o_hi[:, half, :], acc[:]).then_inc(split_step, s.up())
                dve.wait_ge(split_step, s.now())
                dve.tensor_tensor(o_lo[:, half, :], acc[:], o_hi[:, half, :].bitcast(F32),
                                  ALU.subtract).then_inc(acc_copied, 1)

            def first_norm(batch):
                dve.wait_ge(x_in, 16 * (batch + 1))
                layer_norm(xn, xn, xn_ready)

            def residual(batch):
                dve.wait_ge(x_again_in, 16 * (batch + 1))
                for t in range(2):
                    dve.wait_ge(misc_full, m.now() + 1)
                    dve.tensor_tensor(resid[:, 2 * t:2 * t + 2, :].rearrange("p t d -> p (t d)"),
                                      misc[:], resid[:, 2 * t:2 * t + 2, :].rearrange("p t d -> p (t d)"),
                                      ALU.add).then_inc(misc_copied, m.up())

            def second_norm(batch):
                dve.wait_ge(misc_copied, m.now())
                layer_norm(norm, resid, norm_ready)

            def gate_logits(batch):
                dve.wait_ge(misc_full, m.now() + 1)
                dve.tensor_copy(logits[:, :, at(batch), :],
                                misc[:, 0:TT * E].rearrange("p (t o e) -> p t o e", o=1, e=E)
                                ).then_inc(misc_copied, m.up())

            def step_beside(prep, half, batch, done, post):
                split_ctx(prep, 0)
                attention_out(done, half)
                for kc in range(NCH):
                    if kc:
                        split_ctx(prep, kc)
                    key_chunk(prep, kc)
                    value_chunk(prep, half, kc)
                if half == 0:
                    first_norm(batch)
                    dve.wait_ge(x_again_in, 16 * batch)
                    for k in range(KC):
                        two_parts(nt_hi[:, k, :], nt_lo[:, k, :])
                query_chunk(prep)
                if post is not None:
                    residual(post)
                    second_norm(post)
                    for k in range(KC):
                        two_parts(nt_hi[:, k, :], nt_lo[:, k, :])
                    gate_logits(post)

            first_norm(0)
            dve.wait_ge(attn_w_in, 32)
            raw = probs[:, 0, :, :].rearrange("p w (k d) -> p w k d", k=KC)
            dve.tensor_copy(w_hi[:], raw).then_inc(w_split, 1)
            dve.tensor_copy(gate_hi[:], gate_raw[:]).then_inc(w_split, 1)
            dve.wait_ge(w_split, 2)
            dve.tensor_tensor(w_lo[:], raw, w_hi[:].bitcast(F32), ALU.subtract).then_inc(w_split, 1)
            dve.tensor_tensor(gate_lo[:], gate_raw[:], gate_hi[:].bitcast(F32), ALU.subtract
                              ).then_inc(w_split, 1)
            split_ctx(0, 0)
            for k in range(KC):
                two_parts(nt_hi[:, k, :], nt_lo[:, k, :])
            query_chunk(0)
            key_chunk(0, 0)
            dve.wait_ge(const_ready, CONSTS)
            value_chunk(0, 0, 0)
            for kc in range(1, NCH):
                split_ctx(0, kc)
                key_chunk(0, kc)
                value_chunk(0, 0, kc)
            query_chunk(1)
            for kc in range(NCH):
                split_ctx(1, kc)
                key_chunk(1, kc)
                value_chunk(1, 1, kc)
            dve.tensor_scalar(part_batch[:], part_iota[:], 4, None, ALU.logical_shift_right
                              ).then_inc(w_split, 1)
            dve.wait_ge(w_split, 5)
            dve.tensor_scalar(row_base_i[:], part_batch[:], 9, None, ALU.logical_shift_left
                              ).then_inc(w_split, 1)
            dve.wait_ge(w_split, 6)
            dve.tensor_copy(row_base[:], row_base_i[:]).then_inc(w_split, 1)

            s_before, ln_before = s.n, ln.n
            assert m.n == MISC_LOOP
            with dve.Fori(0, B - 1) as i:
                m.base, m.n = i * MISC_TURN + MISC_LOOP, 0
                s.base, s.n = i * SPLIT_TURN + s_before, 0
                ln.base, ln.n = i * LN_TURN + ln_before, 0
                step_beside(2 * i + 2, 0, i + 1, 2 * i, None)
                step_beside(2 * i + 3, 1, i + 1, 2 * i + 1, i)
                assert (m.n, s.n, ln.n) == (MISC_TURN, SPLIT_TURN, LN_TURN)
            m.base, m.n = MISC_LOOP + (B - 1) * MISC_TURN, 0
            s.base, s.n = s_before + (B - 1) * SPLIT_TURN, 0
            ln.base, ln.n = ln_before + (B - 1) * LN_TURN, 0
            attention_out(STEPS - 2, 0)
            attention_out(STEPS - 1, 1)
            residual(B - 1)
            second_norm(B - 1)

            h = Count()
            c = Count()
            tc = Count()
            ts = Count()

            def hidden_quarters(n, par, quarters):
                for f in quarters:
                    now = FT * n + f + 1
                    dve.wait_ge(u_full, now)
                    dve.wait_ge(gelu_done, now)
                    dve.tensor_tensor(hidden[:, f % 2, :], gelu[:, f % 2, :], u_bank[:, f % 2, :],
                                      ALU.mult).then_inc(hidden_done, 1)
                    dve.wait_ge(hidden_done, now)
                    if f == 0:
                        wait_past(dve, d_full, 2 * n - 2)
                    dve.tensor_copy(hid_hi[par][:, f, :], hidden[:, f % 2, :]
                                    ).then_inc(hid_split, 1)
                    dve.wait_ge(hid_split, 2 * now - 1)
                    dve.tensor_tensor(hid_lo[par][:, f, :], hidden[:, f % 2, :],
                                      hid_hi[par][:, f, :].bitcast(F32), ALU.subtract
                                      ).then_inc(hid_split, 1)

            def shared_result(n):
                par = n % 2
                dve.wait_ge(resid_read[par], 16 * (n // 2 + 1))
                if n >= 2:
                    dve.wait_ge(shared_out[par], 16 * (n // 2))
                for t in range(2):
                    dve.wait_ge(d_full, 2 * n + t + 1)
                    two = slice(2 * t, 2 * t + 2)
                    dve.tensor_tensor(result[par][:, two, :].rearrange("p t d -> p (t d)"),
                                      d_bank[:, t, :],
                                      resid_in[par][:, two, :].rearrange("p t d -> p (t d)"),
                                      ALU.add).then_inc(d_copied, 1)

            def expert_result(e, par):
                n = e + B
                dve.wait_ge(shared_out[par], SHARED_OUT)
                wait_past(dve, added[par], 8 * TT * (e - par))
                dve.tensor_copy(add_w[par][:], slot_w[:, :, at(e)].rearrange("p t o -> p (t o)")
                                ).then_inc(adds_ready, 1)
                dve.tensor_copy(add_row[par][:], slot_row[:, :, at(e)].rearrange("p t o -> p (t o)")
                                ).then_inc(adds_ready, 1)
                dve.wait_ge(adds_ready, 2 * e + 1)
                for t in range(TT):
                    dve.wait_ge(d_full, 2 * n + t // 2 + 1)
                    last = dve.tensor_scalar(result[par][:, t, :],
                                             d_bank[:, t // 2, D * (t % 2):D * (t % 2 + 1)],
                                             add_w[par][:, t:t + 1], None, ALU.mult)
                    if t % 2:
                        last.then_inc(d_copied, 1)

            def rows_of(e, par, before):
                if before:
                    dve.wait_ge(rows_in[par], 8 * TT * (e - par))
                dve.tensor_copy(gather_row[par][:], slot_row[:, :, at(e)].rearrange("p t o -> p (t o)")
                                ).then_inc(rows_ready, 1)

            def tokens(par):
                for k in range(KC):
                    dve.wait_ge(tok_full, tc.now() + 1)
                    dve.tensor_copy(tok_hi[par][:, k, :], t_bank[k][:]).then_inc(tok_step, ts.up())
                    dve.wait_ge(tok_step, ts.now())
                    dve.tensor_tensor(tok_lo[par][:, k, :], t_bank[k][:],
                                      tok_hi[par][:, k, :].bitcast(F32), ALU.subtract
                                      ).then_inc(tok_copied, tc.up())

            flat = "p t b e -> p (t b) e"

            def soft_max():
                dve.wait_ge(misc_copied, m.now())
                dve.tensor_reduce(row_max[:], logits[:].rearrange(flat), AX_X, ALU.max
                                  ).then_inc(soft_step, c.up())
                dve.wait_ge(soft_step, c.now())
                dve.tensor_tensor(logits[:].rearrange(flat), logits[:].rearrange(flat),
                                  row_max[:].unsqueeze(2).to_broadcast([P, TT * B, E]), ALU.subtract
                                  ).then_inc(soft_step, c.up())
                assert c.n == SOFT_SUB

            def soft_sum():
                dve.wait_ge(exp_done, 1)
                exps = logits[:].rearrange(flat)
                quarter = exps[:, :, 0:4]
                for i in range(1, E // 4):
                    dve.tensor_tensor(sum4[:], quarter, exps[:, :, 4 * i:4 * i + 4], ALU.add
                                      ).then_inc(soft_step, c.up())
                    dve.wait_ge(soft_step, c.now())
                    quarter = sum4[:]
                dve.tensor_tensor(sum2[:], sum4[:, :, 0::2], sum4[:, :, 1::2], ALU.add
                                  ).then_inc(soft_step, c.up())
                dve.wait_ge(soft_step, c.now())
                dve.tensor_tensor(row_sum[:], sum2[:, :, 0], sum2[:, :, 1], ALU.add
                                  ).then_inc(soft_step, c.up())
                dve.wait_ge(soft_step, c.now())
                dve.reciprocal(row_inv[:], row_sum[:]).then_inc(soft_step, c.up())
                dve.wait_ge(soft_step, c.now())
                dve.tensor_tensor(exps, exps, row_inv[:].unsqueeze(2).to_broadcast([P, TT * B, E]),
                                  ALU.mult).then_inc(soft_step, c.up())
                assert c.n == SOFT_DONE

            def choose(rounds):
                for r in rounds:
                    dve.wait_ge(soft_step, c.now())
                    best, index = top_w[:, 0, 8 * r:8 * r + 8], top_i[:, 8 * r:8 * r + 8]
                    dve.max(best, choice[:]).then_inc(soft_step, c.up())
                    dve.wait_ge(soft_step, c.now())
                    dve.max_index(index, best, choice[:]).then_inc(soft_step, c.up())
                    dve.wait_ge(soft_step, c.now())
                    dve.match_replace(choice[:], best, choice[:], -1.0).then_inc(soft_step, c.up())

            def choice_rows():
                dve.wait_ge(soft_step, c.now())
                for i in range(2):
                    dve.tensor_scalar(top_row[:, i, :], top_i[:], row_base[:], None, ALU.add
                                      ).then_inc(soft_step, c.up())
                dve.tensor_copy(top_w[:, 1, :], top_w[:, 0, :]).then_inc(soft_step, c.up())
                assert c.n == CHOICE_DONE

            def slot_tables():
                for i, to in enumerate((slot_row, slot_w)):
                    dve.wait_ge(tok_full, tc.now() + 1)
                    for odd in range(2):
                        rows = slice(CAP * odd, CAP * (odd + 1))
                        of = t_bank[i][rows, 0:P].rearrange("p (t o e) -> p t o e", o=2, e=E)
                        last = dve.tensor_copy(to[rows, :, :], of[:, :, odd, :])
                    last.then_inc(tok_copied, tc.up())
                dve.wait_ge(tok_copied, tc.now())

            for n in range(B):
                par = n % 2
                hidden_quarters(n, par, (0, 1))
                if n == 1:
                    gate_logits(B - 1)
                if n == 2:
                    soft_sum()
                if n == 3:
                    dve.wait_ge(tok_full, 1)
                    dve.tensor_copy(choice[:], t_bank[0][:]).then_inc(tok_copied, tc.up())
                    dve.wait_ge(tok_copied, 1)
                if n:
                    shared_result(n - 1)
                if n == 6:
                    slot_tables()
                    rows_of(0, 0, False)
                    rows_of(1, 1, False)
                if n == B - 1:
                    tokens(0)
                hidden_quarters(n, par, (2, 3))
                if n == 0:
                    for k in range(KC):
                        two_parts(nt_hi[:, k, :], nt_lo[:, k, :])
                if n == 1:
                    soft_max()
                if 3 <= n <= 5:
                    choose(((0, 1, 2), (3, 4, 5), (6, 7))[n - 3])
                if n == 5:
                    choice_rows()

            def expert(e, par, more_tokens, more_rows):
                n = e + B
                hidden_quarters(n, par, (0, 1))
                if more_tokens:
                    tokens(1 - par)
                if more_rows:
                    rows_of(e + 2, par, True)
                if isinstance(e, int) and e == 0:
                    shared_result(B - 1)
                else:
                    expert_result(e - 1, 1 - par)
                hidden_quarters(n, par, (2, 3))

            expert(0, 0, True, True)
            expert(1, 1, True, True)
            tc0, ts0 = tc.n, ts.n
            with dve.Fori(0, (E - 4) // 2) as i:
                tc.base, tc.n = i * (2 * KC) + tc0, 0
                ts.base, ts.n = i * (2 * KC) + ts0, 0
                expert(2 * i + 2, 0, True, True)
                expert(2 * i + 3, 1, True, True)
            tc.base, tc.n = tc0 + (E - 4) * KC, 0
            ts.base, ts.n = ts0 + (E - 4) * KC, 0
            expert(E - 2, 0, True, False)
            expert(E - 1, 1, False, False)
            expert_result(E - 1, 1)

        @block.tensor
        def _(pe):
            m = Count()

            def into_misc(emit):
                wait_past(pe, misc_copied, m.now())
                emit().then_inc(misc_full, m.up())

            def key_product(prep, half, kc):
                _, n, _ = chunk_of(kc)
                pe.wait_ge(ctx_split, 2 * NCH * prep + 2 * kc + 2)

                def emit():
                    for j, (a, b) in enumerate(PRODUCTS):
                        for k in range(KC):
                            mm = pe.matmul(misc[:, 0:n], W2[a][:, WK, k, P * half:P * (half + 1)],
                                           (ctx_hi, ctx_lo)[b][:, k, 0:n],
                                           start=(j == 0 and k == 0), stop=(j == 2 and k == KC - 1))
                    return mm
                into_misc(emit)

            def value_product(half, kc):
                _, _, tiles = chunk_of(kc)

                def emit():
                    for i, st in enumerate(tiles):
                        n = key_rows(st)
                        for j, (a, b) in enumerate(PRODUCTS):
                            for k in range(KC):
                                mm = pe.matmul(misc[0:n, P * i:P * (i + 1)],
                                               (ctx_hi, ctx_lo)[a][:, k, P * i:P * i + n],
                                               W2[b][:, WV, k, P * half:P * (half + 1)],
                                               start=(j == 0 and k == 0),
                                               stop=(j == 2 and k == KC - 1))
                    return mm
                into_misc(emit)

            def query_product(half):
                def emit():
                    for j, (a, b) in enumerate(PRODUCTS):
                        for k in range(KC):
                            mm = pe.matmul(misc[:], W2[a][:, WQ, k, P * half:P * (half + 1)],
                                           (nt_hi, nt_lo)[b][:, k, :],
                                           start=(j == 0 and k == 0), stop=(j == 2 and k == KC - 1))
                    return mm
                into_misc(emit)

            def transposed(tile, k, ready, count):
                pe.wait_ge(ready, count)

                def emit():
                    for t in range(TT):
                        mm = pe.transpose(misc[:, P * t:P * (t + 1)], tile[:, t, P * k:P * (k + 1)],
                                          ident[:])
                    return mm
                into_misc(emit)

            def out_product(batch, t2):
                pe.wait_ge(acc_copied, 2 * (batch + 1))

                def emit():
                    for t in range(2 * t2, 2 * t2 + 2):
                        for j, (a, b) in enumerate(PRODUCTS):
                            for g in range(2):
                                mm = pe.matmul(misc[:, D * (t % 2):D * (t % 2 + 1)],
                                               (o_hi, o_lo)[a][:, g, P * t:P * (t + 1)],
                                               W2[b][:, WO, g, :],
                                               start=(j == 0 and g == 0), stop=(j == 2 and g == 1))
                    return mm
                into_misc(emit)

            def gate_product():
                def emit():
                    for t in range(TT):
                        for j, (a, b) in enumerate(PRODUCTS):
                            for k in range(KC):
                                mm = pe.matmul(misc[:, E * t:E * (t + 1)],
                                               (nt_hi, nt_lo)[a][:, k, P * t:P * (t + 1)],
                                               (gate_hi, gate_lo)[b][:, k, :],
                                               start=(j == 0 and k == 0),
                                               stop=(j == 2 and k == KC - 1))
                    return mm
                into_misc(emit)

            def beside(prep, half, batch, post):
                when = {1: 0, 4: 1, 7: 2, 10: 3}
                if half == 0:
                    tasks = {16: lambda: transposed(xn, 0, xn_ready, batch + 1),
                             17: lambda: transposed(xn, 1, xn_ready, batch + 1),
                             19: lambda: query_product(half)}
                else:
                    tasks = {12: lambda: query_product(half),
                             14: lambda: out_product(post, 0),
                             15: lambda: out_product(post, 1),
                             20: lambda: transposed(norm, 0, norm_ready, post + 1),
                             21: lambda: transposed(norm, 1, norm_ready, post + 1),
                             24: gate_product}
                for q, kc in when.items():
                    tasks[q] = lambda kc=kc: key_product(prep, half, kc)
                    tasks[q + 1] = lambda kc=kc: value_product(half, kc)
                return tasks

            def weighted_sum(step, half, q):
                st, e = divmod(q, 2)
                n = key_rows(st)
                pe.wait_ge(probs_done, GROUPS * step + 2 * q + 2)
                if q == 0:
                    wait_past(pe, acc_copied, step)
                for c in range(4):
                    mm = pe.matmul(acc[32 * c:32 * (c + 1), :], values[half][0:n, st, c, e, :],
                                   probs[0:n, probs_slot(half, q), c, :],
                                   start=(q == 0), stop=(q == QUADS - 1))
                mm.then_inc(quad_done, 1)

            def attention(step, half, batch, tasks, before=True, by_chunks=False):
                pe.wait_ge(keys_in[half], STACK_DMAS if by_chunks else keys_loaded(half, batch + 1))
                pe.wait_ge(queries_in[half], STACK_DMAS * (batch + 1))
                for q in range(QUADS):
                    st, e = divmod(q, 2)
                    n = key_rows(st)
                    chunk, first = divmod(P * st, CHUNK)
                    if by_chunks and q and first == 0 and e == 0:
                        pe.wait_ge(keys_in[half], STACK_DMAS * (chunk + 1))
                    for pair in range(2):
                        k = 2 * q + pair
                        apart = 2 if half == 1 and k < 2 else 3
                        wait_past(pe, probs_done, GROUPS * step + k - apart + 1)
                        for j in range(2):
                            head = 2 * (2 * pair + j) + e
                            mm = pe.matmul(score[score_slot(half, k)][0:n, j, :],
                                           keys[half][:, head, P * st:P * st + n],
                                           queries[half][:, head, :], start=True, stop=True)
                        mm.then_inc(scores_done, 1)
                    if q >= LAG:
                        weighted_sum(step, half, q - LAG)
                    elif before:
                        weighted_sum(step - 1, 1 - half, QUADS - LAG + q)
                    if q in tasks:
                        tasks[q]()

            pe.wait_ge(const_ready, IDENTITY)
            for k in range(KC):
                transposed(xn, k, xn_ready, 1)
            pe.wait_ge(w_split, 4)
            query_product(0)
            key_product(0, 0, 0)
            value_product(0, 0)
            tasks = {7: lambda: query_product(1)}
            for q, prep, kc in ((0, 0, 1), (3, 0, 2), (5, 0, 3), (9, 1, 0), (12, 1, 1), (14, 1, 2), (17, 1, 3)):
                tasks[q] = lambda prep=prep, kc=kc: key_product(prep, prep, kc)
                tasks[q + 1] = lambda prep=prep, kc=kc: value_product(prep, kc)
            attention(0, 0, 0, tasks, before=False, by_chunks=True)
            with pe.Fori(0, B - 1) as i:
                m.base, m.n = i * MISC_TURN + MISC_LOOP, 0
                attention(2 * i + 1, 1, i, beside(2 * i + 2, 0, i + 1, None))
                attention(2 * i + 2, 0, i + 1, beside(2 * i + 3, 1, i + 1, i))
                assert m.n == MISC_TURN
            m.base, m.n = MISC_LOOP + (B - 1) * MISC_TURN, 0
            attention(STEPS - 1, 1, B - 1, {})
            for q in range(QUADS - LAG, QUADS):
                weighted_sum(STEPS - 1, 1, q)
            for t2 in range(2):
                out_product(B - 1, t2)

            tf = Count()

            def up(n, par, slot, quarters):
                for f in quarters:
                    for w, bank, full in ((0, g_bank, g_full), (1, u_bank, u_full)):
                        wait_past(pe, (gelu_done, hidden_done)[w], FT * n + f - 1)
                        for j, (a, b) in enumerate(PRODUCTS):
                            for k in range(KC):
                                mm = pe.matmul(bank[:, f % 2, :],
                                               (gu_hi, gu_lo)[a][slot][:, w, k, P * f:P * (f + 1)],
                                               (tok_hi, tok_lo)[b][par][:, k, :],
                                               start=(j == 0 and k == 0),
                                               stop=(j == 2 and k == KC - 1))
                        mm.then_inc(full, 1)

            def down(n, par, slot):
                pe.wait_ge(hid_split, 2 * FT * (n + 1))
                for t2 in range(2):
                    wait_past(pe, d_copied, 2 * n + t2 - 1)
                    for t in range(2 * t2, 2 * t2 + 2):
                        for j, (a, b) in enumerate(PRODUCTS):
                            for f in range(FT):
                                mm = pe.matmul(d_bank[:, t2, D * (t % 2):D * (t % 2 + 1)],
                                               (hid_hi, hid_lo)[a][par][:, f, P * t:P * (t + 1)],
                                               (d_hi, d_lo)[b][slot][:, f, :],
                                               start=(j == 0 and f == 0), stop=(j == 2 and f == FT - 1))
                    mm.then_inc(d_full, 1)

            def transpose_rows(e, par):
                pe.wait_ge(rows_in[par], 8 * TT * (e - par) + 16 * TT)
                for k in range(KC):
                    pe.wait_ge(tok_copied, tf.now() + 1 - KC)
                    for t in range(TT):
                        mm = pe.transpose(t_bank[k][:, P * t:P * (t + 1)],
                                          gathered[par][:, t, P * k:P * (k + 1)], ident[:])
                    mm.then_inc(tok_full, tf.up())

            pe.wait_ge(set_split, 2)
            for n in range(B):
                par = n % 2
                pe.wait_ge(tok_in[par], 32 * (n // 2 + 1))
                up(n, par, 0, (0, 1))
                if n == 1:
                    gate_product()
                if n == 3:
                    pe.wait_ge(soft_step, SOFT_DONE)
                    for t in range(TT):
                        mm = pe.transpose(t_bank[0][:, P * t:P * (t + 1)],
                                          logits[:, t, :, :].rearrange("p b e -> p (b e)"), ident[:])
                    mm.then_inc(tok_full, tf.up())
                if n:
                    down(n - 1, 1 - par, 0)
                if n == 6:
                    pe.wait_ge(soft_step, CHOICE_DONE)
                    for i, table in enumerate((top_row, top_w)):
                        pe.transpose(t_bank[i][:, 0:P], table[:].rearrange("p i c -> p (i c)"),
                                     ident[:]).then_inc(tok_full, tf.up())
                    assert tf.n == TABLES
                if n == B - 1:
                    pe.wait_ge(tok_copied, TABLES)
                    transpose_rows(0, 0)
                up(n, par, 0, (2, 3))
                if n == 0:
                    for k in range(KC):
                        transposed(norm, k, norm_ready, B)

            def expert(e, par, more):
                n, slot = e + B, 1 - par
                pe.wait_ge(set_split, 2 * e + 3)
                pe.wait_ge(tok_copied, TABLES + KC * e + KC)
                up(n, par, slot, (0, 1))
                if more:
                    transpose_rows(e + 1, 1 - par)
                pe.wait_ge(set_split, 2 * e + 2)
                down(n - 1, 1 - par, 1 - slot)
                up(n, par, slot, (2, 3))

            expert(0, 0, True)
            expert(1, 1, True)
            tf0 = tf.n
            with pe.Fori(0, (E - 4) // 2) as i:
                tf.base, tf.n = i * (2 * KC) + tf0, 0
                expert(2 * i + 2, 0, True)
                expert(2 * i + 3, 1, True)
            tf.base, tf.n = tf0 + (E - 4) * KC, 0
            expert(E - 2, 0, True)
            expert(E - 1, 1, False)
            pe.wait_ge(set_split, 2 * SETS)
            down(UNITS - 1, 1, 0)


LN_OPS = 2 * TT + 3 + 9
LN_TURN = 2 * LN_OPS
SPLIT_TURN = 2 * (2 * NCH + 2 + 1) + KC + KC
IDENTITY, CONSTS = 3, 5
SOFT_SUB = 2
SOFT_DONE = SOFT_SUB + E // 4 - 1 + 4
CHOICE_DONE = SOFT_DONE + 3 * (CAP // 8) + 3
TABLES = 3


def kernel(x, ctx_1024, L0_xattn_Wq, L0_xattn_Wk, L0_xattn_Wv, L0_xattn_Wo, L0_ffn_gate_w,
           L0_ffn_Wg, L0_ffn_Wu, L0_ffn_Wd, L0_ffn_Ws_g, L0_ffn_Ws_u, L0_ffn_Ws_d):
    import numpy as np
    import concourse.bacc as bacc
    from concourse.bass_utils import run_bass_kernel_spmd

    f32 = np.float32
    ctx_t = np.zeros((B, D, TP), f32)
    ctx_t[:, :, :T] = np.asarray(ctx_1024).transpose(0, 2, 1)
    gate_up = [np.stack([np.asarray(g).T, np.asarray(u).T]) for g, u in
               [(L0_ffn_Ws_g, L0_ffn_Ws_u)] + [(L0_ffn_Wg[e], L0_ffn_Wu[e]) for e in range(E)]]
    downs = [np.asarray(d).T for d in [L0_ffn_Ws_d] + [L0_ffn_Wd[e] for e in range(E)]]
    arrays = {
        "x": np.asarray(x).reshape(B * S, D),
        "ctx_t": ctx_t,
        "w_attn": np.stack([np.asarray(w).T for w in (L0_xattn_Wq, L0_xattn_Wk, L0_xattn_Wv, L0_xattn_Wo)]),
        "gate_t": np.asarray(L0_ffn_gate_w).T,
        "w_gu": np.stack(gate_up),
        "w_d": np.stack(downs),
    }
    arrays = {k: np.ascontiguousarray(v) for k, v in arrays.items()}
    nc = bacc.Bacc("TRN2", target_bir_lowering=False, num_devices=1)
    args = [nc.dram_tensor(k, v.shape, mybir.dt.from_np(v.dtype), kind="ExternalInput").ap()
            for k, v in arrays.items()]
    out = nc.dram_tensor("out", (B * S, D), F32, kind="ExternalOutput").ap()
    build(nc, *args, out)
    r = run_bass_kernel_spmd(nc, [arrays], core_ids=[0])
    return r.results[0]["out"].reshape(B, S, D)
```
